# Optimizing a Trainium2 kernel written in Bass

```python
import numpy as np
import jax
import jax.numpy as jnp

def _softmax(x, axis=-1):
    return jax.nn.softmax(x, axis=axis)

def _gelu(x):
    return jax.nn.gelu(x, approximate=True)

def _silu(x):
    return jax.nn.silu(x)

def _sigmoid(x):
    return jax.nn.sigmoid(x)

def _layernorm(x, axis=-1, eps=1e-05):
    m = jnp.mean(x, axis=axis, keepdims=True)
    v = jnp.var(x, axis=axis, keepdims=True)
    return (x - m) / jnp.sqrt(v + eps)

def _scatter_add(tgt, idx, src, axis=0):
    return tgt.at[idx].add(src)

def _segment_sum(src, seg, n):
    return jax.ops.segment_sum(src, seg, n)
kernel_name = 'mk_cond_resid_d2_seqx_r2_b2efbb'

def setup_inputs(seed: int=0):
    np.random.seed(seed)
    _w = jnp.asarray

    def _rec_inputs():
        import jax
        import jax.numpy as jnp
        _rk = jax.random.key(seed)
        x = -7.109e-05 + 0.9999 * jax.random.normal(jax.random.fold_in(_rk, 1), (64, 128, 2048), jnp.float32)
        _lenS = 128 - jax.random.randint(jax.random.fold_in(_rk, 7), (64,), 0, max(1, 128 // 4) + 1, jnp.int32)
        _lenS2 = 128 - jax.random.randint(jax.random.fold_in(_rk, 8), (64,), 0, max(1, 128 // 4) + 1, jnp.int32)
        itok_B_0_15 = jax.random.randint(jax.random.fold_in(_rk, 11), (64,), 0, 16, jnp.int32)
        itok_B_3_7 = jax.random.randint(jax.random.fold_in(_rk, 12), (64,), 3, 8, jnp.int32)
        return (x, itok_B_0_15, itok_B_3_7)
    x, itok_B_0_15, itok_B_3_7 = _rec_inputs()

    def _L0_cond_setup():
        import jax, jax.numpy as jnp
        import numpy as np
        B, C, T = (64, 128, 2048)
        S, D = (16, 128)
        key = jax.random.key(seed)
        k1, k2, k3 = jax.random.split(key, 3)
        x = jax.random.normal(k1, (B, C, T), dtype=jnp.float32)
        condition = jax.random.randint(k2, (B,), 0, S, dtype=jnp.int64)
        bound = float(np.sqrt(6.0 / C))
        weights = jax.random.uniform(k3, (S, C, D), dtype=jnp.float32, minval=-bound, maxval=bound)
        return {'x': x, 'condition': condition, 'weights': weights}
    _L0_cond_all = _L0_cond_setup()
    _L0_cond_in = {k: v for k, v in _L0_cond_all.items() if k in ('weights',)}
    del _L0_cond_all

    def _L1_cond_setup():
        import jax, jax.numpy as jnp
        import numpy as np
        RANK = 16
        ALPHA = 16.0
        SCALING = ALPHA / RANK
        N_ADAPTERS = 8
        IN_F = 2048
        OUT_F = 2048
        BATCH = 4
        SEQ = 1024
        key = jax.random.key(seed)
        kx, ka, kb, ki = jax.random.split(key, 4)
        x = jax.random.normal(kx, (BATCH, SEQ, IN_F), dtype=jnp.float32)
        A = jax.random.normal(ka, (N_ADAPTERS, OUT_F, RANK), dtype=jnp.float32) * 0.02
        B = jax.random.normal(kb, (N_ADAPTERS, RANK, IN_F), dtype=jnp.float32) * 0.02
        adapter_ids = jax.random.randint(ki, (BATCH,), 0, N_ADAPTERS, dtype=jnp.int32)
        return {'x': x, 'A': A, 'B': B, 'adapter_ids': adapter_ids}
    _L1_cond_all = _L1_cond_setup()
    _L1_cond_in = {k: v for k, v in _L1_cond_all.items() if k in ('A', 'B')}
    del _L1_cond_all
    return {'x': x, 'itok_B_0_15': itok_B_0_15, 'itok_B_3_7': itok_B_3_7, 'L0_cond_weights': _L0_cond_in['weights'], 'L1_cond_A': _L1_cond_in['A'], 'L1_cond_B': _L1_cond_in['B']}

def reference(x, itok_B_0_15, itok_B_3_7, L0_cond_weights, L1_cond_A, L1_cond_B):
    import jax
    import jax.numpy as jnp

    def _L0_cond_ref(x, condition, weights):
        import jax, jax.numpy as jnp
        import numpy as np
        B, C, T = (64, 128, 2048)
        S, D = (16, 128)
        W = weights[condition]
        return jnp.einsum('bct,bcd->bdt', x, W)

    def _L1_cond_ref(x, A, B, adapter_ids):
        import jax, jax.numpy as jnp
        import numpy as np
        RANK = 16
        ALPHA = 16.0
        SCALING = ALPHA / RANK
        N_ADAPTERS = 8
        IN_F = 2048
        OUT_F = 2048
        BATCH = 4
        SEQ = 1024
        B_sel = B[adapter_ids]
        A_sel = A[adapter_ids]
        Bx = jnp.einsum('bni,bri->bnr', x, B_sel)
        out = jnp.einsum('bnr,bor->bno', Bx, A_sel)
        return out * SCALING
    x = x + _L0_cond_ref(x, itok_B_0_15, L0_cond_weights)
    x = x + _L1_cond_ref(x, L1_cond_A, L1_cond_B, itok_B_3_7)
    return x

_drawn_inputs = setup_inputs


def setup_inputs(seed=0):
    import zlib

    import numpy as np

    out = dict(_drawn_inputs(seed))
    spreads = {}
    factors = {}
    for name, (base, spread) in spreads.items():
        noise = np.random.default_rng([zlib.crc32(name.encode()), seed]).standard_normal(out[name].shape)
        drawn = base * np.exp(spread * noise) if base else spread * noise
        out[name] = jnp.asarray(drawn.astype(out[name].dtype))
    for name, factor in factors.items():
        out[name] = (out[name] * factor).astype(out[name].dtype)
    return out
```

```python
import concourse.bass as bass
from concourse import mybir
from contextlib import ExitStack

F32 = mybir.dt.float32
I32 = mybir.dt.int32


def cond_mix_adapter_kernel(nc, x, condition, adapter, mix_w, up_a, down_b, out):
    ALU = mybir.AluOpType
    N, C, T = x.shape
    S, D = mix_w.shape[1:]
    TILES, R, ADAPTERS, UP = up_a.shape
    P = 128
    CHUNKS = T // P
    Q = P // TILES
    PER_TILE = CHUNKS // TILES
    GROUPS = CHUNKS // 4
    BANK = 512
    SLOTS = 4
    BODIES = N // SLOTS
    Y_BANKS = 3
    bank_of = [n % Y_BANKS for n in range(SLOTS * GROUPS)]
    bank_of[-1] = 1

    def bank_user_before(n):
        m = n - 1
        while bank_of[m % len(bank_of)] != bank_of[n]:
            m -= 1
        return n - m

    def wait(engine, sem, value):
        if not isinstance(value, int) or value > 0:
            engine.wait_ge(sem, value)

    with ExitStack() as ctx:
        def sb(name, shape, dt=F32):
            return ctx.enter_context(nc.sbuf_tensor(name, shape, dt))

        def sem(name):
            return ctx.enter_context(nc.semaphore(name))

        x_sb = [sb(f"x_sb{s}", [C, T]) for s in range(SLOTS)]
        y_sb = [sb(f"y_sb{s}", [P, CHUNKS * D]) for s in range(SLOTS)]
        cond_sb = sb("cond_sb", [1, N], I32)
        adapter_sb = sb("adapter_sb", [1, N], I32)
        w_all = sb("w_all", [C, S * D])
        b_all = sb("b_all", [P, ADAPTERS * CHUNKS * R])
        a_all = sb("a_all", [P, ADAPTERS * UP])
        w_sel = [sb(f"w_sel{s}", [C, D]) for s in range(2)]
        b_sel = [sb(f"b_sel{s}", [P, CHUNKS, Q]) for s in range(2)]
        a_sel = [sb(f"a_sel{s}", [P, UP]) for s in range(2)]
        ident = sb("ident", [P, P])
        spread = sb("spread", [P, P])
        part_sb = sb("part_sb", [P, D])
        v_sb = sb("v_sb", [P, D])

        y_ps = [ctx.enter_context(nc.psum_tensor(f"y_ps{i}", [P, BANK], F32)) for i in range(Y_BANKS)]
        up_ps = ctx.enter_context(nc.psum_tensor("up_ps", [P, TILES, BANK], F32))
        v_ps = ctx.enter_context(nc.psum_tensor("v_ps", [P, BANK], F32))
        part_cols, v_cols = v_ps[:, 0:D], v_ps[:, D:2 * D]

        index_loaded = sem("index_loaded")
        w_loaded = sem("w_loaded")
        b_loaded = sem("b_loaded")
        a_loaded = sem("a_loaded")
        x_loaded = [sem(f"x_loaded{s}") for s in range(SLOTS)]
        z_stored = [sem(f"z_stored{s}") for s in range(SLOTS)]
        a_cleared = sem("a_cleared")
        built = sem("built")
        w_ready = sem("w_ready")
        b_ready = sem("b_ready")
        a_ready = sem("a_ready")
        y_made = sem("y_made")
        y_kept = sem("y_kept")
        part_made = sem("part_made")
        part_kept = sem("part_kept")
        v_made = sem("v_made")
        v_kept = sem("v_kept")
        up_made = sem("up_made")
        z_done = sem("z_done")

        block = ctx.enter_context(nc.Block())

        @block.sync
        def _(sp):
            def load(b, slot, body):
                wait(sp, y_made, GROUPS * (b - SLOTS + 1))
                sp.dma_start(x_sb[slot][:, :], x[b, :, :]).then_inc(x_loaded[slot], 16)

            def store(b, slot):
                sp.wait_ge(z_done, b + 1)
                sp.dma_start(out[b, :, :], y_sb[slot][:, :]).then_inc(z_stored[slot], 16)

            sp.dma_start(cond_sb[:, :], condition).then_inc(index_loaded, 16)
            sp.dma_start(adapter_sb[:, :], adapter).then_inc(index_loaded, 16)
            sp.dma_start(w_all[:, :], mix_w.rearrange("c s d -> c (s d)")).then_inc(w_loaded, 16)
            load(0, 0, 0)
            load(1, 1, 0)
            sp.dma_start(b_all[:, :], down_b.rearrange("p a k r -> p (a k r)")).then_inc(b_loaded, 16)
            sp.wait_ge(a_cleared, 1)
            for t in range(TILES):
                sp.dma_start(a_all[Q * t:Q * t + R, :],
                             up_a[t, :, :, :].rearrange("r a n -> r (a n)")).then_inc(a_loaded, 16)
            for b in range(2, SLOTS + 1):
                load(b, b % SLOTS, b // SLOTS)
            with sp.Fori(0, BODIES - 2) as i:
                for k in range(SLOTS):
                    b = i * SLOTS + k
                    load(b + SLOTS + 1, (k + 1) % SLOTS, None)
                    store(b, k)
            for b in range(SLOTS * (BODIES - 2), N):
                if b + SLOTS + 1 < N:
                    load(b + SLOTS + 1, (b + 1) % SLOTS, None)
                store(b, b % SLOTS)
            for s in range(SLOTS):
                sp.wait_ge(z_stored[s], 16 * BODIES)

        @block.gpsimd
        def _(pool):
            def select(b, slot):
                s = slot % 2
                which = pool.value_load(cond_sb[0:1, bass.ds(b, 1)], min_val=0, max_val=S - 1)
                wait(pool, y_made, GROUPS * (b - 1))
                nc.gpsimd.tensor_tensor(w_sel[s][:, :], w_all[:, bass.ds(which * D, D)], ident[:, :],
                                        ALU.add).then_inc(w_ready, 1)
                which = pool.value_load(adapter_sb[0:1, bass.ds(b, 1)], min_val=0, max_val=ADAPTERS - 1)
                wait(pool, part_made, b - 1)
                if isinstance(b, int) and b == 0:
                    pool.wait_ge(b_loaded, 16)
                nc.gpsimd.tensor_copy(
                    b_sel[s][:, :, 0:R],
                    b_all[:, bass.ds(which * (CHUNKS * R), CHUNKS * R)].rearrange("p (k r) -> p k r", r=R),
                ).then_inc(b_ready, 1)
                wait(pool, up_made, b - 1)
                if isinstance(b, int) and b == 0:
                    pool.wait_ge(a_loaded, 16 * TILES)
                nc.gpsimd.tensor_copy(a_sel[s][:, :], a_all[:, bass.ds(which * UP, UP)]).then_inc(a_ready, 1)

            nc.gpsimd.memset(ident[:, :], 0.0).then_inc(built, 1)
            nc.gpsimd.memset(spread[:, :], 0.0).then_inc(built, 1)
            for s in range(2):
                nc.gpsimd.memset(b_sel[s][:, :, :], 0.0).then_inc(built, 1)
            pool.wait_ge(built, 4)
            nc.gpsimd.affine_select(out=ident[:, :], in_=ident[:, :], compare_op=ALU.not_equal, fill=1.0, base=0,
                                    pattern=[[-1, P]], channel_multiplier=1).then_inc(built, 1)
            for n, diagonal in enumerate(range(1 - TILES, TILES)):
                pool.wait_ge(built, 5 + n)
                nc.gpsimd.affine_select(out=spread[:, :], in_=spread[:, :], compare_op=ALU.not_equal, fill=1.0,
                                        base=Q * diagonal, pattern=[[-1, P]],
                                        channel_multiplier=1).then_inc(built, 1)
            pool.wait_ge(index_loaded, 32)
            pool.wait_ge(w_loaded, 16)
            for b in range(SLOTS):
                select(b, b)
            with pool.Fori(1, BODIES) as i:
                for k in range(SLOTS):
                    select(i * SLOTS + k, k)

        @block.tensor
        def _(pe):
            def mix(b, k, g, landed):
                n = k * GROUPS + g
                if g == 0:
                    pe.wait_ge(w_ready, b + 1)
                    pe.wait_ge(x_loaded[k], landed)
                wait(pe, y_kept, GROUPS * b + g - bank_user_before(n) + 1)
                for j in range(4):
                    c = 4 * g + j
                    last = nc.tensor.matmul(y_ps[bank_of[n]][:, j * D:(j + 1) * D],
                                            x_sb[k][:, c * P:(c + 1) * P], w_sel[k % 2][:, :],
                                            start=True, stop=True)
                last.then_inc(y_made, 1)

            def down(b, k):
                pe.wait_ge(y_kept, GROUPS * (b + 1))
                pe.wait_ge(b_ready, b + 1)
                for q in range(PER_TILE):
                    for t in range(TILES):
                        c = q * TILES + t
                        last = nc.tensor.matmul(part_cols[Q * t:Q * (t + 1), :], b_sel[k % 2][:, c, :],
                                                y_sb[k][:, c * D:(c + 1) * D], start=(q == 0),
                                                stop=(q == PER_TILE - 1), tile_position=(0, Q * t))
                last.then_inc(part_made, 1)

            def total(b):
                pe.wait_ge(part_kept, b + 1)
                nc.tensor.matmul(v_cols, spread[:, :], part_sb[:, :], start=True, stop=True).then_inc(v_made, 1)

            def up(b, k):
                pe.wait_ge(v_kept, b + 1)
                pe.wait_ge(a_ready, b + 1)
                wait(pe, z_done, b)
                for q in range(PER_TILE):
                    for t in range(TILES):
                        last = nc.tensor.matmul(up_ps[:, t, q * D:(q + 1) * D],
                                                a_sel[k % 2][Q * t:Q * t + R, q * P:(q + 1) * P],
                                                v_sb[Q * t:Q * t + R, :], start=True, stop=True,
                                                tile_position=(Q * t, 0))
                last.then_inc(up_made, 1)

            def step(b, k, landed, first=False):
                before = (k - 1) % SLOTS
                mix(b, k, 0, landed)
                if not first:
                    down(b - 1, before)
                mix(b, k, 1, landed)
                if not first:
                    total(b - 1)
                mix(b, k, 2, landed)
                if not first:
                    up(b - 1, before)
                mix(b, k, 3, landed)

            pe.wait_ge(built, 5 + 2 * TILES - 1)
            for b in range(SLOTS):
                step(b, b, 16, first=(b == 0))
            with pe.Fori(1, BODIES) as i:
                for k in range(SLOTS):
                    step(i * SLOTS + k, k, i * 16 + 16)
            down(N - 1, SLOTS - 1)
            total(N - 1)
            up(N - 1, SLOTS - 1)

        @block.scalar
        def _(act):
            def keep(b, k, stored):
                for g in range(GROUPS):
                    n = k * GROUPS + g
                    if g == 0:
                        wait(act, z_stored[k], stored)
                    act.wait_ge(y_made, GROUPS * b + g + 1)
                    nc.scalar.copy(y_sb[k][:, g * BANK:(g + 1) * BANK], y_ps[bank_of[n]][:, :]).then_inc(y_kept, 1)

            for b in range(SLOTS):
                keep(b, b, 0)
            with act.Fori(1, BODIES) as i:
                for k in range(SLOTS):
                    keep(i * SLOTS + k, k, i * 16)

        @block.vector
        def _(dve):
            def finish(b, k):
                dve.wait_ge(part_made, b + 1)
                nc.vector.tensor_copy(part_sb[:, :], part_cols).then_inc(part_kept, 1)
                dve.wait_ge(v_made, b + 1)
                nc.vector.tensor_copy(v_sb[:, :], v_cols).then_inc(v_kept, 1)
                dve.wait_ge(up_made, b + 1)
                nc.vector.tensor_tensor(y_sb[k][:, :], y_sb[k][:, :], up_ps[:, :, :].rearrange("p t n -> p (t n)"),
                                        ALU.add).then_inc(z_done, 1)

            nc.vector.memset(a_all[:, :], 0.0).then_inc(a_cleared, 1)
            with dve.Fori(0, BODIES) as i:
                for k in range(SLOTS):
                    finish(i * SLOTS + k, k)


def kernel(x, itok_B_0_15, itok_B_3_7, L0_cond_weights, L1_cond_A, L1_cond_B):
    import numpy as np
    import concourse.bacc as bacc
    from concourse.bass_utils import run_bass_kernel_spmd

    x, cond, adapter, w, a, b = (np.asarray(v) for v in (
        x, itok_B_0_15, itok_B_3_7, L0_cond_weights, L1_cond_A, L1_cond_B))
    n, c, t = x.shape
    s, _, d = w.shape
    adapters, _, r = a.shape
    p, tiles = 128, 4
    arrays = {
        "x": np.ascontiguousarray(x),
        "condition": cond.reshape(1, n),
        "adapter": adapter.reshape(1, n),
        "mix_w": np.ascontiguousarray(w.transpose(1, 0, 2)),
        "up_a": np.ascontiguousarray(a.reshape(adapters, tiles, t // tiles, r).transpose(1, 3, 0, 2)),
        "down_b": np.ascontiguousarray(b.reshape(adapters, r, t // p, p).transpose(3, 0, 2, 1)),
    }
    nc = bacc.Bacc("TRN2", target_bir_lowering=False, num_devices=1)
    args = [nc.dram_tensor(f"in_{name}", v.shape, mybir.dt.from_np(v.dtype), kind="ExternalInput").ap()
            for name, v in arrays.items()]
    out = nc.dram_tensor("out_z", (n, p, t // p * d), F32, kind="ExternalOutput").ap()
    cond_mix_adapter_kernel(nc, *args, out)
    ran = run_bass_kernel_spmd(nc, [{f"in_{name}": v for name, v in arrays.items()}], core_ids=[0])
    z = ran.results[0]["out_z"]
    return z.reshape(n, p, t // p, d).transpose(0, 3, 2, 1).reshape(n, d, t)
```

```python
import concourse.bass as bass
from concourse import mybir
from contextlib import ExitStack

F32 = mybir.dt.float32
BF16 = mybir.dt.bfloat16
I32 = mybir.dt.int32

V_TERM = [1, 1, 1, 2, 2, 2, 3, 3]
A_TERM = [1, 2, 3, 1, 2, 3, 1, 2]


def cond_mix_adapter_kernel(nc, x, condition, adapter, mix_w, up_a, down_b, out):
    ALU = mybir.AluOpType
    N, C, T = x.shape
    S, D = mix_w.shape[1:]
    P, ADAPTERS, CHUNKS, R = up_a.shape
    TILES = 4
    Q = P // TILES
    TERMS = P // R
    GROUPS = CHUNKS // 4
    BANK = 512
    SLOTS = 4
    BODIES = N // SLOTS
    Y_BANKS = 3
    PARTS = 2
    bank_of = [n % Y_BANKS for n in range(SLOTS * GROUPS)]
    bank_of[-1] = 1

    def bank_user_before(n):
        m = n - 1
        while bank_of[m % len(bank_of)] != bank_of[n]:
            m -= 1
        return n - m

    def wait(engine, sem, value):
        if not isinstance(value, int) or value > 0:
            engine.wait_ge(sem, value)

    with ExitStack() as ctx:
        def sb(name, shape, dt=F32):
            return ctx.enter_context(nc.sbuf_tensor(name, shape, dt))

        def sem(name):
            return ctx.enter_context(nc.semaphore(name))

        x_sb = [sb(f"x_sb{s}", [C, T]) for s in range(SLOTS)]
        y_sb = [sb(f"y_sb{s}", [P, CHUNKS * D]) for s in range(SLOTS)]
        cond_sb = sb("cond_sb", [1, N], I32)
        adapter_sb = sb("adapter_sb", [1, N], I32)
        w_all = sb("w_all", [C, S * D])
        b_all = sb("b_all", [P, ADAPTERS * CHUNKS * R])
        a_all = sb("a_all", [P, ADAPTERS * CHUNKS, R])
        a_rest = sb("a_rest", [P, ADAPTERS * CHUNKS, R])
        a_terms = sb("a_terms", [P, ADAPTERS * CHUNKS, TERMS, R], BF16)
        a_stack = sb("a_stack", [P, ADAPTERS, T], BF16)
        w_sel = [sb(f"w_sel{s}", [C, D]) for s in range(2)]
        b_sel = [sb(f"b_sel{s}", [P, CHUNKS, Q]) for s in range(2)]
        a_sel = [sb(f"a_sel{s}", [P, T], BF16) for s in range(2)]
        ident = sb("ident", [P, P])
        ident_bf = sb("ident_bf", [P, P], BF16)
        spread = sb("spread", [P, P])
        minus_v1 = sb("minus_v1", [P, 1])
        minus_v2 = sb("minus_v2", [P, 1])
        part_sb = sb("part_sb", [P, D])
        v_first = sb("v_first", [P, D], BF16)
        v_rest = sb("v_rest", [P, D])
        v_second = sb("v_second", [P, D], BF16)
        v_terms = sb("v_terms", [P, D], BF16)

        y_ps = [ctx.enter_context(nc.psum_tensor(f"y_ps{i}", [P, BANK], F32)) for i in range(Y_BANKS)]
        up_ps = ctx.enter_context(nc.psum_tensor("up_ps", [P, CHUNKS * D], F32))
        v_ps = ctx.enter_context(nc.psum_tensor("v_ps", [P, BANK], F32))
        part_cols, v_cols = v_ps[:, 0:D], v_ps[:, D:2 * D]
        HALF = CHUNKS * D // 2
        stack_ps = [up_ps[:, h * HALF:(h + 1) * HALF].bitcast(BF16) for h in range(2)]

        index_loaded = sem("index_loaded")
        w_loaded = sem("w_loaded")
        b_loaded = sem("b_loaded")
        a_loaded = sem("a_loaded")
        x_loaded = [sem(f"x_loaded{s}") for s in range(SLOTS)]
        z_stored = [sem(f"z_stored{s}") for s in range(SLOTS)]
        built = sem("built")
        filled = sem("filled")
        first_term = sem("first_term")
        rest_made = sem("rest_made")
        second_term = sem("second_term")
        third_term = sem("third_term")
        terms_dve = sem("terms_dve")
        terms_act = sem("terms_act")
        turned = sem("turned")
        stacked_dve = sem("stacked_dve")
        stacked_act = sem("stacked_act")
        w_ready = sem("w_ready")
        b_ready = sem("b_ready")
        a_ready = sem("a_ready")
        y_made = sem("y_made")
        y_kept = sem("y_kept")
        part_made = sem("part_made")
        part_kept = sem("part_kept")
        v_made = sem("v_made")
        v_step = sem("v_step")
        v_split = sem("v_split")
        up_made = sem("up_made")
        z_done = sem("z_done")

        block = ctx.enter_context(nc.Block())

        @block.sync
        def _(sp):
            def load(b, slot):
                wait(sp, y_made, GROUPS * (b - SLOTS + 1))
                sp.dma_start(x_sb[slot][:, :], x[b, :, :]).then_inc(x_loaded[slot], 16)

            def store(b, slot):
                sp.wait_ge(z_done, b + 1)
                sp.dma_start(out[b, :, :], y_sb[slot][:, :]).then_inc(z_stored[slot], 16)

            sp.dma_start(cond_sb[:, :], condition).then_inc(index_loaded, 16)
            sp.dma_start(adapter_sb[:, :], adapter).then_inc(index_loaded, 16)
            sp.dma_start(w_all[:, :], mix_w.rearrange("c s d -> c (s d)")).then_inc(w_loaded, 16)
            sp.dma_start(a_all[:, :, :], up_a.rearrange("p a k r -> p (a k) r")).then_inc(a_loaded, 16)
            load(0, 0)
            sp.dma_start(b_all[:, :], down_b.rearrange("p a k r -> p (a k r)")).then_inc(b_loaded, 16)
            for b in range(1, SLOTS + 1):
                load(b, b % SLOTS)
            with sp.Fori(0, BODIES - 2) as i:
                for k in range(SLOTS):
                    b = i * SLOTS + k
                    load(b + SLOTS + 1, (k + 1) % SLOTS)
                    store(b, k)
            for b in range(SLOTS * (BODIES - 2), N):
                if b + SLOTS + 1 < N:
                    load(b + SLOTS + 1, (b + 1) % SLOTS)
                store(b, b % SLOTS)
            for s in range(SLOTS):
                sp.wait_ge(z_stored[s], 16 * BODIES)

        @block.gpsimd
        def _(pool):
            def select_w(b, s):
                which = pool.value_load(cond_sb[0:1, bass.ds(b, 1)], min_val=0, max_val=S - 1)
                wait(pool, y_made, GROUPS * (b - 1))
                nc.gpsimd.tensor_tensor(w_sel[s][:, :], w_all[:, bass.ds(which * D, D)], ident[:, :],
                                        ALU.add).then_inc(w_ready, 1)

            def select_b(b, s):
                which = pool.value_load(adapter_sb[0:1, bass.ds(b, 1)], min_val=0, max_val=ADAPTERS - 1)
                wait(pool, part_made, b - 1)
                nc.gpsimd.tensor_copy(
                    b_sel[s][:, :, 0:R],
                    b_all[:, bass.ds(which * (CHUNKS * R), CHUNKS * R)].rearrange("p (k r) -> p k r", r=R),
                ).then_inc(b_ready, 1)

            def diagonal(m, base, signal):
                nc.gpsimd.affine_select(out=m[:, :], in_=m[:, :], compare_op=ALU.not_equal, fill=1.0, base=base,
                                        pattern=[[-1, P]], channel_multiplier=1).then_inc(signal, 1)

            nc.gpsimd.memset(ident[:, :], 0.0).then_inc(built, 1)
            nc.gpsimd.memset(ident_bf[:, :], 0.0).then_inc(built, 1)
            pool.wait_ge(built, 2)
            diagonal(ident, 0, built)
            diagonal(ident_bf, 0, built)
            pool.wait_ge(built, 4)
            pool.wait_ge(index_loaded, 32)
            pool.wait_ge(w_loaded, 16)
            select_w(0, 0)
            select_w(1, 1)
            nc.gpsimd.memset(spread[:, :], 0.0).then_inc(filled, 1)
            nc.gpsimd.memset(minus_v1[:, :], 0.0).then_inc(filled, 1)
            nc.gpsimd.memset(minus_v2[:, :], 0.0).then_inc(filled, 1)
            for s in range(2):
                nc.gpsimd.memset(b_sel[s][:, :, :], 0.0).then_inc(filled, 1)
            pool.wait_ge(filled, 5)
            for m, term in ((minus_v1, 2), (minus_v2, 3)):
                nc.gpsimd.affine_select(out=m[:, :], in_=m[:, :], compare_op=ALU.is_gt, fill=-1.0,
                                        base=R * V_TERM.index(term), pattern=[[0, 1]],
                                        channel_multiplier=-1).then_inc(filled, 1)
            for n in range(1 - TERMS, TERMS):
                diagonal(spread, R * n, filled)
                pool.wait_ge(filled, 7 + n + TERMS)
            pool.wait_ge(b_loaded, 16)
            select_b(0, 0)
            select_b(1, 1)
            for b in range(2, SLOTS):
                select_w(b, b % 2)
                select_b(b, b % 2)
            with pool.Fori(1, BODIES) as i:
                for k in range(SLOTS):
                    select_w(i * SLOTS + k, k % 2)
                    select_b(i * SLOTS + k, k % 2)

        FILLED = 7 + 2 * TERMS - 1

        @block.tensor
        def _(pe):
            def mix(b, k, g, landed):
                n = k * GROUPS + g
                if g == 0:
                    pe.wait_ge(w_ready, b + 1)
                    pe.wait_ge(x_loaded[k], landed)
                wait(pe, y_kept, GROUPS * b + g - bank_user_before(n) + 1)
                for j in range(4):
                    c = 4 * g + j
                    last = nc.tensor.matmul(y_ps[bank_of[n]][:, j * D:(j + 1) * D],
                                            x_sb[k][:, c * P:(c + 1) * P], w_sel[k % 2][:, :],
                                            start=True, stop=True)
                last.then_inc(y_made, 1)

            def down(b, k):
                pe.wait_ge(y_kept, GROUPS * (b + 1))
                pe.wait_ge(b_ready, b + 1)
                wait(pe, v_split, b)
                for q in range(CHUNKS // TILES):
                    for t in range(TILES):
                        c = q * TILES + t
                        last = nc.tensor.matmul(part_cols[Q * t:Q * (t + 1), :], b_sel[k % 2][:, c, :],
                                                y_sb[k][:, c * D:(c + 1) * D], start=(q == 0),
                                                stop=(q == CHUNKS // TILES - 1), tile_position=(0, Q * t))
                last.then_inc(part_made, 1)

            def total(b):
                pe.wait_ge(part_kept, b + 1)
                nc.tensor.matmul(v_cols, spread[:, :], part_sb[:, :], start=True, stop=True).then_inc(v_made, 1)

            def up(b, k):
                pe.wait_ge(v_split, b + 1)
                pe.wait_ge(a_ready, b + 1)
                wait(pe, z_done, b)
                for c in range(CHUNKS):
                    last = nc.tensor.matmul(up_ps[:, c * D:(c + 1) * D], a_sel[k % 2][:, c * P:(c + 1) * P],
                                            v_terms[:, :], start=True, stop=True)
                last.then_inc(up_made, 1)

            def turn():
                for a in range(ADAPTERS):
                    if a % (ADAPTERS // PARTS) == 0:
                        part = a // (ADAPTERS // PARTS)
                        pe.wait_ge(terms_dve, part + 1)
                        pe.wait_ge(terms_act, part + 1)
                    wait(pe, (stacked_dve, stacked_act)[a % 2], a // 2)
                    for c in range(CHUNKS):
                        last = nc.tensor.transpose(
                            stack_ps[a % 2][:, c * P:(c + 1) * P],
                            a_terms[:, a * CHUNKS + c, :, :].rearrange("p j r -> p (j r)"), ident_bf[:, :])
                    last.then_inc(turned, 1)
                pe.wait_ge(stacked_dve, ADAPTERS // 2)
                pe.wait_ge(stacked_act, ADAPTERS // 2)

            def step(b, k, landed, first=False, second=False):
                before = (k - 1) % SLOTS
                mix(b, k, 0, landed)
                if not first:
                    down(b - 1, before)
                mix(b, k, 1, landed)
                if not first:
                    total(b - 1)
                mix(b, k, 2, landed)
                mix(b, k, 3, landed)
                if second:
                    turn()
                if not first:
                    up(b - 1, before)

            pe.wait_ge(built, 4)
            step(0, 0, 16, first=True)
            pe.wait_ge(filled, FILLED)
            step(1, 1, 16, second=True)
            for b in range(2, SLOTS):
                step(b, b, 16)
            with pe.Fori(1, BODIES) as i:
                for k in range(SLOTS):
                    step(i * SLOTS + k, k, i * 16 + 16)
            down(N - 1, SLOTS - 1)
            total(N - 1)
            up(N - 1, SLOTS - 1)

        LOT = ADAPTERS * CHUNKS // PARTS

        @block.scalar
        def _(act):
            def keep(b, k, stored):
                for g in range(GROUPS):
                    n = k * GROUPS + g
                    if g == 0:
                        wait(act, z_stored[k], stored)
                    act.wait_ge(y_made, GROUPS * b + g + 1)
                    nc.scalar.copy(y_sb[k][:, g * BANK:(g + 1) * BANK], y_ps[bank_of[n]][:, :]).then_inc(y_kept, 1)

            for part in range(PARTS):
                lot = slice(part * LOT, (part + 1) * LOT)
                first, *more = [j for j in range(TERMS) if A_TERM[j] == 1]
                act.wait_ge(first_term, part + 1)
                for j in more:
                    last = nc.scalar.copy(a_terms[:, lot, j, :], a_terms[:, lot, first, :])
                last.then_inc(terms_act, 1)
            keep(0, 0, 0)
            keep(1, 1, 0)
            for a in range(1, ADAPTERS, 2):
                act.wait_ge(turned, a + 1)
                nc.scalar.copy(a_stack[:, a, :], stack_ps[1]).then_inc(stacked_act, 1)
            for b in range(2, SLOTS):
                keep(b, b, 0)
            with act.Fori(1, BODIES) as i:
                for k in range(SLOTS):
                    keep(i * SLOTS + k, k, i * 16)

        @block.vector
        def _(dve):
            def split_a(part):
                lot = slice(part * LOT, (part + 1) * LOT)
                groups = [[j for j in range(TERMS) if A_TERM[j] == term] for term in (1, 2, 3)]
                a1, a2, a3 = (a_terms[:, lot, g[0], :] for g in groups)
                nc.vector.tensor_copy(a1, a_all[:, lot, :]).then_inc(first_term, 1)
                dve.wait_ge(first_term, part + 1)
                nc.vector.tensor_tensor(a_rest[:, lot, :], a_all[:, lot, :], a1, ALU.subtract).then_inc(rest_made, 1)
                dve.wait_ge(rest_made, part + 1)
                nc.vector.tensor_copy(a2, a_rest[:, lot, :]).then_inc(second_term, 1)
                dve.wait_ge(second_term, part + 1)
                nc.vector.tensor_tensor(a3, a_rest[:, lot, :], a2, ALU.subtract).then_inc(third_term, 1)
                for j in groups[1][1:]:
                    nc.vector.tensor_copy(a_terms[:, lot, j, :], a2)
                dve.wait_ge(third_term, part + 1)
                for j in groups[2][1:]:
                    last = nc.vector.tensor_copy(a_terms[:, lot, j, :], a3)
                last.then_inc(terms_dve, 1)

            def split_v(b):
                dve.wait_ge(part_made, b + 1)
                nc.vector.tensor_copy(part_sb[:, :], part_cols).then_inc(part_kept, 1)
                dve.wait_ge(v_made, b + 1)
                nc.vector.tensor_copy(v_first[:, :], v_cols).then_inc(v_step, 1)
                dve.wait_ge(v_step, 3 * b + 1)
                nc.vector.scalar_tensor_tensor(out=v_rest[:, :], in0=v_first[:, :], scalar=minus_v1[:, 0:1],
                                               in1=v_cols, op0=ALU.mult, op1=ALU.add).then_inc(v_step, 1)
                dve.wait_ge(v_step, 3 * b + 2)
                nc.vector.tensor_copy(v_second[:, :], v_rest[:, :]).then_inc(v_step, 1)
                dve.wait_ge(v_step, 3 * b + 3)
                nc.vector.scalar_tensor_tensor(out=v_terms[:, :], in0=v_second[:, :], scalar=minus_v2[:, 0:1],
                                               in1=v_rest[:, :], op0=ALU.mult, op1=ALU.add).then_inc(v_split, 1)

            def pick_a(b, s):
                which = dve.value_load(adapter_sb[0:1, bass.ds(b, 1)], min_val=0, max_val=ADAPTERS - 1)
                nc.vector.tensor_copy(a_sel[s][:, :], a_flat[:, bass.ds(which * T, T)]).then_inc(a_ready, 1)

            def finish(b, k):
                dve.wait_ge(up_made, b + 1)
                nc.vector.tensor_tensor(y_sb[k][:, :], y_sb[k][:, :], up_ps[:, :], ALU.add).then_inc(z_done, 1)

            a_flat = a_stack[:, :, :].rearrange("p a n -> p (a n)")
            dve.wait_ge(a_loaded, 16)
            for part in range(PARTS):
                split_a(part)
            dve.wait_ge(filled, FILLED)
            split_v(0)
            for a in range(0, ADAPTERS, 2):
                dve.wait_ge(turned, a + 1)
                nc.vector.tensor_copy(a_stack[:, a, :], stack_ps[0]).then_inc(stacked_dve, 1)
            dve.wait_ge(index_loaded, 32)
            dve.wait_ge(stacked_dve, ADAPTERS // 2)
            dve.wait_ge(stacked_act, ADAPTERS // 2)
            pick_a(0, 0)
            pick_a(1, 1)
            finish(0, 0)
            for b in range(1, SLOTS):
                split_v(b)
                pick_a(b + 1, (b + 1) % 2)
                finish(b, b)
            with dve.Fori(1, BODIES - 1) as i:
                for k in range(SLOTS):
                    split_v(i * SLOTS + k)
                    pick_a(i * SLOTS + k + 1, (k + 1) % 2)
                    finish(i * SLOTS + k, k)
            for b in range(N - SLOTS, N):
                split_v(b)
                if b + 1 < N:
                    pick_a(b + 1, (b + 1) % 2)
                finish(b, b % SLOTS)


def kernel(x, itok_B_0_15, itok_B_3_7, L0_cond_weights, L1_cond_A, L1_cond_B):
    import numpy as np
    import concourse.bacc as bacc
    from concourse.bass_utils import run_bass_kernel_spmd

    x, cond, adapter, w, a, b = (np.asarray(v) for v in (
        x, itok_B_0_15, itok_B_3_7, L0_cond_weights, L1_cond_A, L1_cond_B))
    n, c, t = x.shape
    s, _, d = w.shape
    adapters, _, r = a.shape
    p = 128
    arrays = {
        "x": np.ascontiguousarray(x),
        "condition": cond.reshape(1, n),
        "adapter": adapter.reshape(1, n),
        "mix_w": np.ascontiguousarray(w.transpose(1, 0, 2)),
        "up_a": np.ascontiguousarray(a.reshape(adapters, t // p, p, r).transpose(2, 0, 1, 3)),
        "down_b": np.ascontiguousarray(b.reshape(adapters, r, t // p, p).transpose(3, 0, 2, 1)),
    }
    nc = bacc.Bacc("TRN2", target_bir_lowering=False, num_devices=1)
    args = [nc.dram_tensor(f"in_{name}", v.shape, mybir.dt.from_np(v.dtype), kind="ExternalInput").ap()
            for name, v in arrays.items()]
    out = nc.dram_tensor("out_z", (n, p, t // p * d), F32, kind="ExternalOutput").ap()
    cond_mix_adapter_kernel(nc, *args, out)
    ran = run_bass_kernel_spmd(nc, [{f"in_{name}": v for name, v in arrays.items()}], core_ids=[0])
    z = ran.results[0]["out_z"]
    return z.reshape(n, p, t // p, d).transpose(0, 3, 2, 1).reshape(n, d, t)
```

```python
import concourse.bass as bass
from concourse import mybir
from contextlib import ExitStack

F32 = mybir.dt.float32
BF16 = mybir.dt.bfloat16
I32 = mybir.dt.int32

V_TERM = [1, 1, 1, 2, 2, 2, 3, 3]
A_TERM = [1, 2, 3, 1, 2, 3, 1, 2]


def cond_mix_adapter_kernel(nc, x, condition, adapter, mix_w, up_a, down_b, out):
    ALU = mybir.AluOpType
    N, C, T = x.shape
    S, D = mix_w.shape[1:]
    P, ADAPTERS, CHUNKS, R = up_a.shape
    TILES = 4
    Q = P // TILES
    TERMS = P // R
    GROUPS = CHUNKS // 4
    BANK = 512
    SLOTS = 4
    BODIES = N // SLOTS
    LEAD = SLOTS + 2
    WHOLE = N - 2
    Y_BANKS = 3
    PARTS = 2
    bank_of = [n % Y_BANKS for n in range(SLOTS * GROUPS)]
    bank_of[-1] = 1

    def bank_user_before(n):
        m = n - 1
        while bank_of[m % len(bank_of)] != bank_of[n]:
            m -= 1
        return n - m

    def banks_before(b):
        return WHOLE + (b - WHOLE) * GROUPS

    def wait(engine, sem, value):
        if not isinstance(value, int) or value > 0:
            engine.wait_ge(sem, value)

    with ExitStack() as ctx:
        def sb(name, shape, dt=F32):
            return ctx.enter_context(nc.sbuf_tensor(name, shape, dt))

        def sem(name):
            return ctx.enter_context(nc.semaphore(name))

        x_sb = [sb(f"x_sb{s}", [C, T]) for s in range(SLOTS)]
        y_sb = [sb(f"y_sb{s}", [P, CHUNKS * D]) for s in range(SLOTS)]
        cond_sb = sb("cond_sb", [1, N], I32)
        adapter_sb = sb("adapter_sb", [1, N], I32)
        w_all = sb("w_all", [C, S * D])
        w_first = [sb(f"w_first{b}", [C, D]) for b in range(SLOTS)]
        b_all = sb("b_all", [P, ADAPTERS * CHUNKS * R])
        a_all = sb("a_all", [P, ADAPTERS * CHUNKS, R])
        a_rest = sb("a_rest", [P, ADAPTERS * CHUNKS, R])
        a_terms = sb("a_terms", [P, ADAPTERS * CHUNKS, TERMS, R], BF16)
        a_terms_flat = a_terms[:, :, :, :].rearrange("p m j r -> p (m j r)").bitcast(F32)
        z_sb = [a_terms_flat[:, s * T:(s + 1) * T] for s in range(SLOTS)]
        a_stack = sb("a_stack", [P, ADAPTERS, T], BF16)
        w_sel = [sb(f"w_sel{s}", [C, D]) for s in range(2)]
        b_sel = [sb(f"b_sel{s}", [P, CHUNKS * R]) for s in range(2)]
        a_sel = [sb(f"a_sel{s}", [P, T], BF16) for s in range(2)]
        ident = sb("ident", [P, P])
        ident_bf = sb("ident_bf", [P, P], BF16)
        spread = sb("spread", [P, TERMS, R])
        minus_v1 = sb("minus_v1", [P, 1])
        minus_v2 = sb("minus_v2", [P, 1])
        part_sb = sb("part_sb", [P, D])
        v_first = sb("v_first", [P, D], BF16)
        v_rest = sb("v_rest", [P, D])
        v_second = sb("v_second", [P, D], BF16)
        v_terms = [sb(f"v_terms{s}", [P, D], BF16) for s in range(2)]

        y_ps = [ctx.enter_context(nc.psum_tensor(f"y_ps{i}", [P, BANK], F32)) for i in range(Y_BANKS)]
        up_ps = ctx.enter_context(nc.psum_tensor("up_ps", [P, CHUNKS * D], F32))
        v_ps = ctx.enter_context(nc.psum_tensor("v_ps", [P, BANK], F32))
        part_cols, v_cols = v_ps[:, 0:D], v_ps[:, D:2 * D]
        HALF = CHUNKS * D // 2
        stack_ps = [up_ps[:, h * HALF:(h + 1) * HALF].bitcast(BF16) for h in range(2)]

        index_loaded = sem("index_loaded")
        w_loaded = sem("w_loaded")
        w_first_loaded = [sem(f"w_first_loaded{b}") for b in range(SLOTS)]
        b_loaded = sem("b_loaded")
        a_loaded = sem("a_loaded")
        x_loaded = [sem(f"x_loaded{s}") for s in range(SLOTS)]
        z_stored = [sem(f"z_stored{s}") for s in range(SLOTS)]
        last_stored = [sem(f"last_stored{g}") for g in range(GROUPS)]
        part_cleared = sem("part_cleared")
        built = sem("built")
        filled = sem("filled")
        first_term = sem("first_term")
        rest_made = sem("rest_made")
        second_term = sem("second_term")
        third_term = sem("third_term")
        terms_dve = sem("terms_dve")
        terms_act = sem("terms_act")
        turned = sem("turned")
        stacked_dve = sem("stacked_dve")
        stacked_act = sem("stacked_act")
        w_ready = sem("w_ready")
        b_ready = sem("b_ready")
        a_ready = sem("a_ready")
        y_made = sem("y_made")
        y_kept = sem("y_kept")
        part_made = sem("part_made")
        part_kept = sem("part_kept")
        v_made = sem("v_made")
        v_step = sem("v_step")
        v_split = sem("v_split")
        up_made = sem("up_made")
        z_done = sem("z_done")

        block = ctx.enter_context(nc.Block())

        @block.sync
        def _(sp):
            def load(b, slot):
                wait(sp, y_made, GROUPS * (b - SLOTS + 1))
                sp.dma_start(x_sb[slot][:, :], x[b, :, :]).then_inc(x_loaded[slot], 16)

            def load_w(b):
                which = sp.value_load(cond_sb[0:1, b:b + 1], min_val=0, max_val=S - 1)
                sp.dma_start(w_first[b][:, :], mix_w[:, bass.ds(which, 1), :].rearrange("c s d -> c (s d)")
                             ).then_inc(w_first_loaded[b], 16)

            def store(b, slot):
                sp.wait_ge(z_done, b + 1)
                sp.dma_start(out[b, :, :], z_sb[slot]).then_inc(z_stored[slot], 16)

            sp.dma_start(cond_sb[:, :], condition).then_inc(index_loaded, 16)
            sp.dma_start(adapter_sb[:, :], adapter).then_inc(index_loaded, 16)
            load(0, 0)
            sp.wait_ge(index_loaded, 32)
            load_w(0)
            sp.dma_start(a_all[:, :, :], up_a.rearrange("p a k r -> p (a k) r")).then_inc(a_loaded, 16)
            load_w(1)
            load(1, 1)
            sp.dma_start(b_all[:, :], down_b.rearrange("p a k r -> p (a k r)")).then_inc(b_loaded, 16)
            for b in range(2, SLOTS):
                load_w(b)
                load(b, b)
            sp.dma_start(w_all[:, :], mix_w.rearrange("c s d -> c (s d)")).then_inc(w_loaded, 16)
            for b in range(SLOTS, LEAD):
                load(b, b % SLOTS)
            with sp.Fori(0, BODIES - 2) as i:
                for k in range(SLOTS):
                    b = i * SLOTS + k
                    load(b + LEAD, (k + LEAD) % SLOTS)
                    store(b, k)
            for b in range(SLOTS * (BODIES - 2), WHOLE):
                if b + LEAD < N:
                    load(b + LEAD, (b + LEAD) % SLOTS)
                store(b, b % SLOTS)
            for b in range(WHOLE, N):
                for g in range(GROUPS):
                    cols = slice(g * BANK, (g + 1) * BANK)
                    sp.wait_ge(z_done, banks_before(b) + g + 1)
                    sp.dma_start(out[b, :, cols], z_sb[b % SLOTS][:, cols]).then_inc(last_stored[g], 16)
            for s in range(SLOTS):
                sp.wait_ge(z_stored[s], 16 * len(range(s, WHOLE, SLOTS)))
            for g in range(GROUPS):
                sp.wait_ge(last_stored[g], 16 * (N - WHOLE))

        @block.gpsimd
        def _(pool):
            def select_w(b, s):
                which = pool.value_load(cond_sb[0:1, bass.ds(b, 1)], min_val=0, max_val=S - 1)
                wait(pool, y_made, GROUPS * (b - 1))
                nc.gpsimd.tensor_tensor(w_sel[s][:, :], w_all[:, bass.ds(which * D, D)], ident[:, :],
                                        ALU.add).then_inc(w_ready, 1)

            def select_b(b, s):
                which = pool.value_load(adapter_sb[0:1, bass.ds(b, 1)], min_val=0, max_val=ADAPTERS - 1)
                wait(pool, part_made, b - 1)
                nc.gpsimd.tensor_copy(b_sel[s][:, :],
                                      b_all[:, bass.ds(which * (CHUNKS * R), CHUNKS * R)]).then_inc(b_ready, 1)

            def first_w(b):
                pool.wait_ge(w_first_loaded[b], 16)
                wait(pool, y_made, GROUPS * (b - 1))
                nc.gpsimd.tensor_tensor(w_sel[b % 2][:, :], w_first[b][:, :], ident[:, :],
                                        ALU.add).then_inc(w_ready, 1)

            def diagonal(m):
                nc.gpsimd.affine_select(out=m[:, :], in_=m[:, :], compare_op=ALU.not_equal, fill=1.0, base=0,
                                        pattern=[[-1, P]], channel_multiplier=1).then_inc(built, 1)

            nc.gpsimd.memset(ident[:, :], 0.0).then_inc(built, 1)
            nc.gpsimd.memset(ident_bf[:, :], 0.0).then_inc(built, 1)
            pool.wait_ge(built, 2)
            diagonal(ident)
            diagonal(ident_bf)
            pool.wait_ge(built, 4)
            first_w(0)
            first_w(1)
            nc.gpsimd.memset(spread[:, :, :], 0.0).then_inc(filled, 1)
            nc.gpsimd.memset(minus_v1[:, :], 0.0).then_inc(filled, 1)
            nc.gpsimd.memset(minus_v2[:, :], 0.0).then_inc(filled, 1)
            pool.wait_ge(filled, 3)
            for m, term in ((minus_v1, 2), (minus_v2, 3)):
                nc.gpsimd.affine_select(out=m[:, :], in_=m[:, :], compare_op=ALU.is_gt, fill=-1.0,
                                        base=R * V_TERM.index(term), pattern=[[0, 1]],
                                        channel_multiplier=-1).then_inc(filled, 1)
            for n in range(TERMS):
                nc.gpsimd.affine_select(out=spread[:, :, :], in_=spread[:, :, :], compare_op=ALU.not_equal, fill=1.0,
                                        base=-R * n, pattern=[[0, TERMS], [-1, R]],
                                        channel_multiplier=1).then_inc(filled, 1)
                pool.wait_ge(filled, 6 + n)
            pool.wait_ge(index_loaded, 32)
            pool.wait_ge(b_loaded, 16)
            select_b(0, 0)
            select_b(1, 1)
            for b in range(2, SLOTS):
                first_w(b)
                select_b(b, b % 2)
            pool.wait_ge(w_loaded, 16)
            with pool.Fori(1, BODIES) as i:
                for k in range(SLOTS):
                    select_w(i * SLOTS + k, k % 2)
                    select_b(i * SLOTS + k, k % 2)

        FILLED = 5 + TERMS

        @block.tensor
        def _(pe):
            def mix(b, k, g, landed=None):
                n = k * GROUPS + g
                if g == 0:
                    pe.wait_ge(w_ready, b + 1)
                    pe.wait_ge(x_loaded[k], landed)
                wait(pe, y_kept, GROUPS * b + g - bank_user_before(n) + 1)
                for j in range(4):
                    c = 4 * g + j
                    last = nc.tensor.matmul(y_ps[bank_of[n]][:, j * D:(j + 1) * D],
                                            x_sb[k][:, c * P:(c + 1) * P], w_sel[k % 2][:, :],
                                            start=True, stop=True)
                last.then_inc(y_made, 1)

            def down(b, k):
                pe.wait_ge(y_kept, GROUPS * (b + 1))
                pe.wait_ge(b_ready, b + 1)
                wait(pe, v_step, 3 * b - 1)
                for q in range(CHUNKS // TILES):
                    for t in range(TILES):
                        c = q * TILES + t
                        last = nc.tensor.matmul(part_cols[Q * t:Q * t + R, :], b_sel[k % 2][:, c * R:(c + 1) * R],
                                                y_sb[k][:, c * D:(c + 1) * D], start=(q == 0),
                                                stop=(q == CHUNKS // TILES - 1), tile_position=(0, Q * t))
                last.then_inc(part_made, 1)

            def total(b):
                pe.wait_ge(part_kept, b + 1)
                nc.tensor.matmul(v_cols, spread[:, :, :].rearrange("p j r -> p (j r)"), part_sb[:, :], start=True, stop=True).then_inc(v_made, 1)

            def up_chunk(k, c):
                return nc.tensor.matmul(up_ps[:, c * D:(c + 1) * D], a_sel[k % 2][:, c * P:(c + 1) * P],
                                        v_terms[k % 2][:, :], start=True, stop=True)

            def up(b, k):
                pe.wait_ge(v_split, b + 1)
                pe.wait_ge(a_ready, b + 1)
                wait(pe, z_done, b)
                for c in range(CHUNKS):
                    last = up_chunk(k, c)
                last.then_inc(up_made, 1)

            def up_by_bank(b, k):
                pe.wait_ge(v_split, b + 1)
                pe.wait_ge(a_ready, b + 1)
                pe.wait_ge(z_done, banks_before(b))
                for g in range(GROUPS):
                    for c in range(4 * g, 4 * g + 4):
                        last = up_chunk(k, c)
                    last.then_inc(up_made, 1)

            def turn(a):
                if a % (ADAPTERS // PARTS) == 0:
                    part = a // (ADAPTERS // PARTS)
                    pe.wait_ge(terms_dve, part + 1)
                    pe.wait_ge(terms_act, part + 1)
                wait(pe, stacked_dve, a - 1)
                wait(pe, stacked_act, a - 1)
                for c in range(CHUNKS):
                    last = nc.tensor.transpose(
                        stack_ps[a % 2][:, c * P:(c + 1) * P],
                        a_terms[:, a * CHUNKS + c, :, :].rearrange("p j r -> p (j r)"), ident_bf[:, :])
                last.then_inc(turned, 1)

            def step(b, k, landed):
                mix(b, k, 0, landed)
                down(b - 1, (k - 1) % SLOTS)
                up(b - 2, (k - 2) % SLOTS)
                mix(b, k, 1)
                total(b - 1)
                mix(b, k, 2)
                mix(b, k, 3)

            pe.wait_ge(built, 4)
            for b in range(2):
                for g in range(GROUPS):
                    mix(b, b, g, 16)
            pe.wait_ge(filled, FILLED)
            pe.wait_ge(part_cleared, 1)
            turn(0)
            turn(1)
            down(0, 0)
            mix(2, 2, 0, 16)
            mix(2, 2, 1)
            turn(2)
            turn(3)
            total(0)
            mix(2, 2, 2)
            turn(4)
            turn(5)
            mix(2, 2, 3)
            turn(6)
            turn(7)
            down(1, 1)
            mix(3, 3, 0, 16)
            total(1)
            mix(3, 3, 1)
            pe.wait_ge(stacked_dve, ADAPTERS)
            pe.wait_ge(stacked_act, ADAPTERS)
            up(0, 0)
            down(2, 2)
            mix(3, 3, 2)
            mix(3, 3, 3)
            up(1, 1)
            total(2)
            with pe.Fori(1, BODIES) as i:
                for k in range(SLOTS):
                    step(i * SLOTS + k, k, i * 16 + 16)
            up_by_bank(N - 2, SLOTS - 2)
            down(N - 1, SLOTS - 1)
            total(N - 1)
            up_by_bank(N - 1, SLOTS - 1)

        LOT = ADAPTERS * CHUNKS // PARTS

        groups_of = {term: [j for j in range(TERMS) if A_TERM[j] == term] for term in (1, 2, 3)}

        def lot(part):
            return slice(part * LOT, (part + 1) * LOT)

        @block.scalar
        def _(act):
            def keep(b, k, g):
                if g == 0:
                    wait(act, z_done, b - SLOTS + 1)
                act.wait_ge(y_made, GROUPS * b + g + 1)
                nc.scalar.copy(y_sb[k][:, g * BANK:(g + 1) * BANK],
                               y_ps[bank_of[k * GROUPS + g]][:, :]).then_inc(y_kept, 1)

            def repeat_a1(part):
                act.wait_ge(first_term, part + 1)
                nc.scalar.copy(a_terms[:, lot(part), groups_of[1][1], :],
                               a_terms[:, lot(part), groups_of[1][0], :]).then_inc(terms_act, 1)

            def stack(a):
                act.wait_ge(turned, a + 1)
                nc.scalar.copy(a_stack[:, a, T // 2:T], stack_ps[a % 2][:, T // 2:T]).then_inc(stacked_act, 1)

            keep(0, 0, 0)
            keep(0, 0, 1)
            repeat_a1(0)
            keep(0, 0, 2)
            keep(0, 0, 3)
            keep(1, 1, 0)
            keep(1, 1, 1)
            keep(1, 1, 2)
            keep(1, 1, 3)
            repeat_a1(1)
            stack(0)
            stack(1)
            keep(2, 2, 0)
            keep(2, 2, 1)
            stack(2)
            stack(3)
            keep(2, 2, 2)
            stack(4)
            stack(5)
            keep(2, 2, 3)
            stack(6)
            stack(7)
            for g in range(GROUPS):
                keep(3, 3, g)
            with act.Fori(1, BODIES) as i:
                for k in range(SLOTS):
                    for g in range(GROUPS):
                        keep(i * SLOTS + k, k, g)
            act.wait_ge(part_made, N)
            nc.scalar.copy(part_sb[:, :], part_cols).then_inc(part_kept, 1)

        @block.vector
        def _(dve):
            def split_a(part):
                a1, a2, a3 = (a_terms[:, lot(part), groups_of[term][0], :] for term in (1, 2, 3))
                whole, rest = a_all[:, lot(part), :], a_rest[:, lot(part), :]
                nc.vector.tensor_copy(a1, whole).then_inc(first_term, 1)
                dve.wait_ge(first_term, part + 1)
                nc.vector.tensor_tensor(rest, whole, a1, ALU.subtract).then_inc(rest_made, 1)
                dve.wait_ge(rest_made, part + 1)
                nc.vector.tensor_copy(a2, rest).then_inc(second_term, 1)
                dve.wait_ge(second_term, part + 1)
                nc.vector.tensor_tensor(a3, rest, a2, ALU.subtract).then_inc(third_term, 1)
                nc.vector.tensor_copy(a_terms[:, lot(part), groups_of[1][2], :], a1)
                for j in groups_of[2][1:]:
                    nc.vector.tensor_copy(a_terms[:, lot(part), j, :], a2)
                dve.wait_ge(third_term, part + 1)
                nc.vector.tensor_copy(a_terms[:, lot(part), groups_of[3][1], :], a3).then_inc(terms_dve, 1)

            def keep_part(b):
                dve.wait_ge(part_made, b + 1)
                nc.vector.tensor_copy(part_sb[:, :], part_cols).then_inc(part_kept, 1)

            def split_v(b, s):
                dve.wait_ge(v_made, b + 1)
                nc.vector.tensor_copy(v_first[:, :], v_cols).then_inc(v_step, 1)
                dve.wait_ge(v_step, 3 * b + 1)
                nc.vector.scalar_tensor_tensor(out=v_rest[:, :], in0=v_first[:, :], scalar=minus_v1[:, 0:1],
                                               in1=v_cols, op0=ALU.mult, op1=ALU.add).then_inc(v_step, 1)
                dve.wait_ge(v_step, 3 * b + 2)
                nc.vector.tensor_copy(v_second[:, :], v_rest[:, :]).then_inc(v_step, 1)
                dve.wait_ge(v_step, 3 * b + 3)
                nc.vector.scalar_tensor_tensor(out=v_terms[s][:, :], in0=v_second[:, :], scalar=minus_v2[:, 0:1],
                                               in1=v_rest[:, :], op0=ALU.mult, op1=ALU.add).then_inc(v_split, 1)

            def adapter_of(b):
                return dve.value_load(adapter_sb[0:1, bass.ds(b, 1)], min_val=0, max_val=ADAPTERS - 1)

            def pick_a(which, s):
                nc.vector.tensor_copy(a_sel[s][:, :], a_flat[:, bass.ds(which * T, T)]).then_inc(a_ready, 1)

            def finish(b, k, stored):
                wait(dve, z_stored[k], stored)
                dve.wait_ge(up_made, b + 1)
                nc.vector.tensor_tensor(z_sb[k], y_sb[k][:, :], up_ps[:, :], ALU.add).then_inc(z_done, 1)

            def stack(a):
                dve.wait_ge(turned, a + 1)
                nc.vector.tensor_copy(a_stack[:, a, 0:T // 2], stack_ps[a % 2][:, 0:T // 2]).then_inc(stacked_dve, 1)

            def step(b, k, stored):
                which = adapter_of(b + 2)
                finish(b, k, stored)
                split_v(b + 1, (k + 1) % 2)
                pick_a(which, k % 2)
                keep_part(b + 2)

            a_flat = a_stack[:, :, :].rearrange("p a n -> p (a n)")
            nc.vector.memset(part_cols, 0.0).then_inc(part_cleared, 1)
            dve.wait_ge(index_loaded, 32)
            first = [adapter_of(b) for b in range(SLOTS)]
            dve.wait_ge(a_loaded, 16)
            for part in range(PARTS):
                split_a(part)
            dve.wait_ge(filled, FILLED)
            stack(0)
            stack(1)
            keep_part(0)
            stack(2)
            stack(3)
            split_v(0, 0)
            for a in range(4, ADAPTERS):
                stack(a)
            dve.wait_ge(stacked_dve, ADAPTERS)
            dve.wait_ge(stacked_act, ADAPTERS)
            pick_a(first[0], 0)
            keep_part(1)
            split_v(1, 1)
            pick_a(first[1], 1)
            finish(0, 0, 0)
            pick_a(first[2], 0)
            keep_part(2)
            finish(1, 1, 0)
            split_v(2, 0)
            pick_a(first[3], 1)
            keep_part(3)
            for b in range(2, SLOTS):
                step(b, b, 0)
            with dve.Fori(1, BODIES - 1) as i:
                for k in range(SLOTS):
                    step(i * SLOTS + k, k, i * 16)
            step(N - 4, 0, 16 * (BODIES - 1))
            last = adapter_of(N - 1)
            finish(N - 3, 1, 16 * (BODIES - 1))
            split_v(N - 2, 0)
            pick_a(last, 1)
            for b in range(WHOLE, N):
                if b == N - 1:
                    split_v(b, 1)
                dve.wait_ge(z_stored[b % SLOTS], 16 * (BODIES - 1))
                for g in range(GROUPS):
                    cols = slice(g * BANK, (g + 1) * BANK)
                    dve.wait_ge(up_made, banks_before(b) + g + 1)
                    nc.vector.tensor_tensor(z_sb[b % SLOTS][:, cols], y_sb[b % SLOTS][:, cols], up_ps[:, cols],
                                            ALU.add).then_inc(z_done, 1)


def kernel(x, itok_B_0_15, itok_B_3_7, L0_cond_weights, L1_cond_A, L1_cond_B):
    import numpy as np
    import concourse.bacc as bacc
    from concourse.bass_utils import run_bass_kernel_spmd

    x, cond, adapter, w, a, b = (np.asarray(v) for v in (
        x, itok_B_0_15, itok_B_3_7, L0_cond_weights, L1_cond_A, L1_cond_B))
    n, c, t = x.shape
    s, _, d = w.shape
    adapters, _, r = a.shape
    p = 128
    arrays = {
        "x": np.ascontiguousarray(x),
        "condition": cond.reshape(1, n),
        "adapter": adapter.reshape(1, n),
        "mix_w": np.ascontiguousarray(w.transpose(1, 0, 2)),
        "up_a": np.ascontiguousarray(a.reshape(adapters, t // p, p, r).transpose(2, 0, 1, 3)),
        "down_b": np.ascontiguousarray(b.reshape(adapters, r, t // p, p).transpose(3, 0, 2, 1)),
    }
    nc = bacc.Bacc("TRN2", target_bir_lowering=False, num_devices=1)
    args = [nc.dram_tensor(f"in_{name}", v.shape, mybir.dt.from_np(v.dtype), kind="ExternalInput").ap()
            for name, v in arrays.items()]
    out = nc.dram_tensor("out_z", (n, p, t // p * d), F32, kind="ExternalOutput").ap()
    cond_mix_adapter_kernel(nc, *args, out)
    ran = run_bass_kernel_spmd(nc, [{f"in_{name}": v for name, v in arrays.items()}], core_ids=[0])
    z = ran.results[0]["out_z"]
    return z.reshape(n, p, t // p, d).transpose(0, 3, 2, 1).reshape(n, d, t)
```
